# Optimizing a Trainium2 kernel written in Bass

```python
import numpy as np
import jax
import jax.numpy as jnp

def _softmax(x, axis=-1):
    return jax.nn.softmax(x, axis=axis)

def _gelu(x):
    return jax.nn.gelu(x, approximate=True)

def _silu(x):
    return jax.nn.silu(x)

def _sigmoid(x):
    return jax.nn.sigmoid(x)

def _layernorm(x, axis=-1, eps=1e-05):
    m = jnp.mean(x, axis=axis, keepdims=True)
    v = jnp.var(x, axis=axis, keepdims=True)
    return (x - m) / jnp.sqrt(v + eps)

def _scatter_add(tgt, idx, src, axis=0):
    return tgt.at[idx].add(src)

def _segment_sum(src, seg, n):
    return jax.ops.segment_sum(src, seg, n)
kernel_name = 'mk_seq_preln_d1_jaxref_r4_b50342'

def setup_inputs(seed: int=0):
    np.random.seed(seed)
    _w = jnp.asarray

    def _L0_attn_setup():
        import jax, jax.numpy as jnp
        import numpy as np
        B, C, L = (64, 128, 1024)
        key = jax.random.key(seed)
        x = jax.random.normal(key, (B, C, L), dtype=jnp.float32)
        return {'x': x}
    _L0_attn_in = _L0_attn_setup()

    def _L0_ffn_setup():
        import jax, jax.numpy as jnp
        import numpy as np
        BLOCK = 64
        NF4_CODE = jnp.array([-1.0, -0.6961928009986877, -0.5250730514526367, -0.39491748809814453, -0.28444138169288635, -0.18477343022823334, -0.09105003625154495, 0.0, 0.07958029955625534, 0.16093020141124725, 0.24611230194568634, 0.33791524171829224, 0.44070982933044434, 0.5626170039176941, 0.7229568362236023, 1.0], dtype=jnp.float32)

        def dequant_nf4(q, absmax, shape):
            w = NF4_CODE[q.reshape(-1)]
            w = w.reshape(-1, BLOCK) * absmax[:, None]
            return w.reshape(shape)
        key = jax.random.key(seed)
        ks = jax.random.split(key, 7)
        HD, M = (1024, 3584)
        nblk = HD * M // BLOCK
        x = jax.random.normal(ks[0], (2, 512, HD), dtype=jnp.float32)
        gate_q = jax.random.randint(ks[1], (M, HD), 0, 16, dtype=jnp.int32)
        up_q = jax.random.randint(ks[2], (M, HD), 0, 16, dtype=jnp.int32)
        down_q = jax.random.randint(ks[3], (HD, M), 0, 16, dtype=jnp.int32)
        gate_absmax = jax.random.uniform(ks[4], (nblk,), dtype=jnp.float32) * 0.05
        up_absmax = jax.random.uniform(ks[5], (nblk,), dtype=jnp.float32) * 0.05
        down_absmax = jax.random.uniform(ks[6], (nblk,), dtype=jnp.float32) * 0.05
        return {'x': x, 'gate_q': gate_q, 'gate_absmax': gate_absmax, 'up_q': up_q, 'up_absmax': up_absmax, 'down_q': down_q, 'down_absmax': down_absmax}
    _L0_ffn_in = _L0_ffn_setup()
    _d = {'L0_attn_x': _L0_attn_in['x'], 'L0_ffn_gate_q': _L0_ffn_in['gate_q'], 'L0_ffn_gate_absmax': _L0_ffn_in['gate_absmax'], 'L0_ffn_up_q': _L0_ffn_in['up_q'], 'L0_ffn_up_absmax': _L0_ffn_in['up_absmax'], 'L0_ffn_down_q': _L0_ffn_in['down_q'], 'L0_ffn_down_absmax': _L0_ffn_in['down_absmax']}
    _x0 = _d['L0_attn_x']
    _d['L0_attn_x'] = jax.random.normal(jax.random.fold_in(jax.random.key(seed), 1), (4, 512, 1024), dtype=_x0.dtype)
    del _x0
    return _d

def reference(L0_attn_x, L0_ffn_gate_q, L0_ffn_gate_absmax, L0_ffn_up_q, L0_ffn_up_absmax, L0_ffn_down_q, L0_ffn_down_absmax):

    def _L0_attn_ref(x):
        import jax, jax.numpy as jnp
        import numpy as np
        B, C, L = (64, 128, 1024)
        b, c, l = x.shape
        q = jnp.transpose(x, (2, 0, 1))
        scale = jnp.asarray(c, x.dtype) ** 0.5
        scores = jnp.einsum('lnc,lmc->lnm', q, q) / scale
        prob = jax.nn.softmax(scores, axis=-1)
        msg = jnp.einsum('lnm,lmc->lnc', prob, q)
        return x + jnp.transpose(msg, (1, 2, 0))

    def _L0_ffn_ref(x, gate_q, gate_absmax, up_q, up_absmax, down_q, down_absmax):
        import jax, jax.numpy as jnp
        import numpy as np
        BLOCK = 64
        NF4_CODE = jnp.array([-1.0, -0.6961928009986877, -0.5250730514526367, -0.39491748809814453, -0.28444138169288635, -0.18477343022823334, -0.09105003625154495, 0.0, 0.07958029955625534, 0.16093020141124725, 0.24611230194568634, 0.33791524171829224, 0.44070982933044434, 0.5626170039176941, 0.7229568362236023, 1.0], dtype=jnp.float32)

        def dequant_nf4(q, absmax, shape):
            w = NF4_CODE[q.reshape(-1)]
            w = w.reshape(-1, BLOCK) * absmax[:, None]
            return w.reshape(shape)
        HD = x.shape[-1]
        M = gate_q.shape[0]
        Wg = dequant_nf4(gate_q, gate_absmax, (M, HD))
        Wu = dequant_nf4(up_q, up_absmax, (M, HD))
        Wd = dequant_nf4(down_q, down_absmax, (HD, M))
        g = jnp.einsum('bsh,mh->bsm', x, Wg)
        u = jnp.einsum('bsh,mh->bsm', x, Wu)
        h = jax.nn.silu(g) * u
        return jnp.einsum('bsm,hm->bsh', h, Wd)
    x = L0_attn_x
    x = x + _L0_attn_ref(_layernorm(x, axis=-1))
    x = x + _L0_ffn_ref(_layernorm(x, axis=-1), L0_ffn_gate_q, L0_ffn_gate_absmax, L0_ffn_up_q, L0_ffn_up_absmax, L0_ffn_down_q, L0_ffn_down_absmax)
    return x

_drawn_inputs = setup_inputs


def setup_inputs(seed=0):
    import zlib

    import numpy as np

    out = dict(_drawn_inputs(seed))
    spreads = {}
    factors = {'L0_ffn_gate_absmax': 3.065, 'L0_ffn_up_absmax': 3.103, 'L0_ffn_down_absmax': 3.113}
    for name, (base, spread) in spreads.items():
        noise = np.random.default_rng([zlib.crc32(name.encode()), seed]).standard_normal(out[name].shape)
        drawn = base * np.exp(spread * noise) if base else spread * noise
        out[name] = jnp.asarray(drawn.astype(out[name].dtype))
    for name, factor in factors.items():
        out[name] = (out[name] * factor).astype(out[name].dtype)
    return out
```

```python
import concourse.bass as bass
from concourse import mybir
from contextlib import ExitStack

P = 128
B, C, L = 4, 512, 1024
M = 3584
BLOCK = 64
CT = C // P
TOK = B * P
NJ = CT * B
KT = L // P
LB = L // 32
LG = LB // 4
CM = 2
NCHUNK = M // P // CM
HALF = 512
PAIRS = CM * CT
ADDS = NJ * 2

AHEAD = [(0, 0, 0, 0), (0, 0, 1, 0), (1, 0, 0, 0), (1, 0, 1, 0), (0, 1, 0, 0), (0, 1, 1, 0)]
BODY = [(1, 1, 0, 0), (1, 1, 1, 0),
        (2, 0, 0, 0), (2, 0, 1, 0), (2, 1, 0, 0), (2, 1, 1, 0),
        (0, 0, 0, 1), (0, 0, 1, 1), (1, 0, 0, 1), (1, 0, 1, 1),
        (0, 1, 0, 1), (0, 1, 1, 1)]
NA = len(AHEAD)
NBODY = len(BODY)
NLAST = 6
NHALVES = NA + NBODY * (NCHUNK - 1) + NLAST

LINE_N0 = (0.30380716919898987, 1.1266502141952515)
LINE_N1 = (0.13015556335449219, 0.12570476531982422)
LINE_N2 = (0.09966795146465302, 0.014562472701072693)
SLOPE_67 = 0.09105003625154495
LINE_P0 = (0.08134990185499191, -0.001769602298736572)
LINE_P1 = (0.0918029397726059, -0.029296517372131348)
LINE_P2 = (0.1219071745872498, -0.16882604360580444)
LINE_P3 = (0.2770431637763977, -1.2163453102111816)


def half_at(j):
    return AHEAD[NA + j] if j < 0 else BODY[j]


def n_his(j):
    return 2 if half_at(j)[0] == 2 else 1


HIS_AHEAD = sum(n_his(j) for j in range(-NA, 0))
HIS_BODY = sum(n_his(j) for j in range(NBODY))


def his_until(i, j):
    if j < 0:
        return sum(n_his(t) for t in range(-NA, j + 1))
    return HIS_BODY * i + HIS_AHEAD + sum(n_his(t) for t in range(j + 1))


def number(i, j):
    return NBODY * i + NA + j


def block_kernel(nc: bass.Bass, x, q_stream, a_stream, absmax, out):
    F32, F16, I32 = mybir.dt.float32, mybir.dt.float16, mybir.dt.int32
    ALU = mybir.AluOpType
    ACT = mybir.ActivationFunctionType
    AX = mybir.AxisListType.X

    ctx = ExitStack()
    with ctx:
        def sb(name, shape, dt):
            return ctx.enter_context(nc.sbuf_tensor(name, shape, dt))

        def sem(name):
            return ctx.enter_context(nc.semaphore(name))

        acc = sb("acc", [P, NJ, L], F32)
        blk = sb("blk", [P, CT, B * L], F32)
        h_mem = sb("h_mem", [P, 4096], F32)
        w_mem = sb("w_mem", [P, 3 * 1024 + 2048 + 2048], F32)
        h_hl = h_mem[:, :].bitcast(F16).rearrange("p (m s t) -> p m s t", m=CM, s=2)
        down_w = w_mem[:, 0:3072].bitcast(F16).rearrange("p (m s t) -> p m s t", m=CM, s=3)
        gu_w = [w_mem[:, 5120:7168].bitcast(F16).rearrange("p (g s t) -> p g s t", g=2, s=2),
                w_mem[:, 3072:5120].bitcast(F16).rearrange("p (g s t) -> p g s t", g=2, s=2)]

        q_in = sb("q_in", [P, 2, HALF], I32)
        a_in = sb("a_in", [P, 2, HALF], F32)
        r_buf = sb("r_buf", [P, 2, HALF], F32)
        line = {n: sb(f"line_{n}", [P, HALF], F32) for n in ("N0", "N1", "N2", "P0", "P1", "P2", "P3")}
        w_buf = sb("w_buf", [P, HALF], F32)
        s_buf = sb("s_buf", [P, TOK], F32)

        absmax_sb = h_mem[:, 0:3 * 448].rearrange("p (a b) -> p a b", a=3)
        masked = h_mem[:, :].rearrange("p (g l) -> p g l", l=32)
        d_mat = h_mem[:, :].rearrange("p (b n l) -> p b n l", n=B, l=32)
        y_t = w_mem[:, 0:4096].rearrange("p (b c) -> p b c", c=P)
        xn_buf = w_mem[:, 4096:5120].rearrange("p (s t) -> p s t", s=2)
        rep = w_mem[:, 4096:4608].rearrange("p (n m) -> p n m", n=B)
        y_nat = [blk[:, ct, :].rearrange("p (b n l) -> p b n l", n=B, l=32) for ct in range(CT)]
        xn_t = [blk[:, ct, :].bitcast(F16).rearrange("p (s k t) -> p s k t", s=2, k=KT) for ct in range(CT)]

        ident = sb("ident", [P, P], F32)
        mask32 = sb("mask32", [P, 32], F32)
        same_n = sb("same_n", [P, B], F32)
        stats = sb("stats", [P, B, 2, 6], F32)
        mean_var = sb("mean_var", [P, B, 2], F32)
        var_eps = sb("var_eps", [P, B], F32)
        std = sb("std", [P, B], F32)
        rstd = sb("rstd", [P, B], F32)
        tmp4 = sb("tmp4", [P, B], F32)
        ln_scale = sb("ln_scale", [P, 2, B], F32)
        ln_bias = sb("ln_bias", [P, 2, B], F32)
        scores = sb("scores", [P, LB, B], F32)
        row_stat = sb("row_stat", [P, LB], F32)
        prob = sb("prob", [P, LB, B], F32)
        prob_m = sb("prob_m", [P, LB, B], F32)
        amax = sb("amax", [P, 3], F32)
        amax_all = sb("amax_all", [P, 3], F32)
        pow2 = sb("pow2", [P, 3], F32)
        w_scale = sb("w_scale", [P, 3], F32)
        g_back = sb("g_back", [P, 1], F32)
        u_back = sb("u_back", [P, 1], F32)
        y_back = sb("y_back", [P, 1], F32)

        ps = ctx.enter_context(nc.psum_tensor("ps", [P, 8, 512], F32))
        gram = ps[:, :, :].rearrange("p k (b m l) -> p (k b) m l", m=B, l=32)

        absmax_in = sem("absmax_in")
        x_in = [sem(f"x_in{j}") for j in range(NJ)]
        q_arrived = [sem(f"q_arrived{s}") for s in range(2)]
        a_arrived = [sem(f"a_arrived{s}") for s in range(2)]
        out_done = sem("out_done")
        consts = sem("consts")
        amax_sem = sem("amax_sem")
        amax_red = sem("amax_red")
        v_chain = sem("v_chain")
        var_ready = sem("var_ready")
        std_ready = sem("std_ready")
        ln_ready = sem("ln_ready")
        y_ready = sem("y_ready")
        gram_done = sem("gram_done")
        gram_read = sem("gram_read")
        diff_ready = sem("diff_ready")
        exp_ready = sem("exp_ready")
        prob_ready = sem("prob_ready")
        rep_done = sem("rep_done")
        d_ready = sem("d_ready")
        t_done = sem("t_done")
        t_read = sem("t_read")
        m_done = sem("m_done")
        x1_ready = sem("x1_ready")
        xn_ready = sem("xn_ready")
        t2_done = sem("t2_done")
        xhi_done = sem("xhi_done")
        xlo_done = sem("xlo_done")
        lines_done = sem("lines_done")
        combos_done = sem("combos_done")
        his_done = sem("his_done")
        los_done = sem("los_done")
        gate_ready = sem("gate_ready")
        up_ready = sem("up_ready")
        gate_read = sem("gate_read")
        up_read = sem("up_read")
        hhi_done = sem("hhi_done")
        hlo_done = sem("hlo_done")
        down_ready = sem("down_ready")
        down_added = sem("down_added")

        x_v = x.rearrange("n (t p) l -> t n p l", p=P)
        out_v = out.rearrange("n (t p) l -> t n p l", p=P)
        block = ctx.enter_context(nc.Block())

        @block.sync
        def _(sp):
            def load_half(k, s, wait=None):
                if wait is not None:
                    sp.wait_ge(lines_done, 8 * (wait) + 1)
                sp.dma_start(q_in[:, s, :], q_stream[k, :, :]).then_inc(q_arrived[s], 16)
                if wait is not None:
                    sp.wait_ge(combos_done, 8 * (wait) + 8)
                sp.dma_start(a_in[:, s, :],
                             a_stream[k, :, :].rearrange("(o t) n -> o t n", o=2)
                             .broadcast_to([2, BLOCK, HALF])).then_inc(a_arrived[s], 16)

            for j in range(B):
                sp.dma_start(acc[:, j, :], x_v[0, j]).then_inc(x_in[j], 16)
            sp.dma_start(absmax_sb, absmax.rearrange("a (p b) -> p a b", p=P)).then_inc(absmax_in, 16)
            for k in range(2):
                load_half(k, k)
            for j in range(B, NJ):
                sp.dma_start(acc[:, j, :], x_v[j // B, j % B]).then_inc(x_in[j], 16)
            for k in range(2, NA):
                load_half(k, k % 2, k - 2)
            with sp.Fori(0, NCHUNK - 1) as i:
                for j in range(NBODY):
                    load_half(NBODY * i + NA + j, j % 2, NBODY * i + NA + j - 2)
            for j in range(NLAST):
                k = number(NCHUNK - 1, j)
                load_half(k, k % 2, k - 2)
            for j in range(NJ):
                sp.wait_ge(down_added, ADDS * (NCHUNK - 1) + 2 * j + 2)
                sp.dma_start(out_v[j // B, j % B], acc[:, j, :]).then_inc(out_done, 16)
            sp.wait_ge(out_done, 16 * NJ)

        @block.gpsimd
        def _(pool):
            nc.gpsimd.memset(ident[:, :], 0.0).then_inc(consts, 1)
            nc.gpsimd.memset(mask32[:, :], 0.0).then_inc(consts, 1)
            nc.gpsimd.memset(rep, 0.0).then_inc(consts, 1)
            nc.gpsimd.memset(same_n[:, :], 1.0).then_inc(consts, 1)
            pool.wait_ge(consts, 4)
            nc.gpsimd.affine_select(out=ident[:, :], in_=ident[:, :], compare_op=ALU.not_equal, fill=1.0,
                                    base=0, pattern=[[-1, P]], channel_multiplier=1).then_inc(consts, 1)
            for a in range(4):
                pool.wait_ge(consts, 5 + a)
                nc.gpsimd.affine_select(out=mask32[:, :], in_=mask32[:, :], compare_op=ALU.not_equal,
                                        fill=1.0, base=-32 * a, pattern=[[-1, 32]],
                                        channel_multiplier=1).then_inc(consts, 1)
            rep4 = rep.rearrange("p n (m l) -> p n m l", l=32)
            nc.gpsimd.affine_select(out=rep4, in_=rep4, compare_op=ALU.not_equal, fill=1.0, base=0,
                                    pattern=[[-32, B], [0, 4], [-1, 32]],
                                    channel_multiplier=1).then_inc(consts, 1)
            nc.gpsimd.affine_select(out=same_n[:, :], in_=same_n[:, :], compare_op=ALU.is_ge, fill=0.0,
                                    base=0, pattern=[[-32, B]], channel_multiplier=1).then_inc(consts, 1)
            pool.wait_ge(consts, 11)
            nc.gpsimd.affine_select(out=same_n[:, :], in_=same_n[:, :], compare_op=ALU.is_ge, fill=0.0,
                                    base=31, pattern=[[32, B]], channel_multiplier=-1).then_inc(consts, 1)
            pool.wait_ge(amax_sem, 1)
            nc.gpsimd.partition_all_reduce(amax_all[:, :], amax[:, :], P,
                                           bass.bass_isa.ReduceOp.max).then_inc(amax_red, 1)

        @block.scalar
        def _(act):
            def unpack_lines(i, j):
                k = number(i, j)
                first = isinstance(k, int) and k == 0
                s = (NA + j) % 2
                arrived = 16 * ((NBODY // 2) * i + (NA + j) // 2 + 1)
                act.wait_ge(q_arrived[s], arrived)
                if not (isinstance(k, int) and k < 2):
                    act.wait_ge(combos_done, 8 * k - 11)
                nc.scalar.activation(r_buf[:, s, :], q_in[:, s, :], ACT.Copy,
                                     bias=-7.0, scale=1.0).then_inc(lines_done, 1)
                act.wait_ge(lines_done, 8 * k + 1)
                for name, (slope, at0), used in (("N0", LINE_N0, 1), ("P0", LINE_P0, 2), ("N1", LINE_N1, 3),
                                                 ("P1", LINE_P1, 4), ("P2", LINE_P2, 6), ("N2", LINE_N2, 7)):
                    if not first:
                        act.wait_ge(combos_done, 8 * k - 8 + used)
                    nc.scalar.activation(line[name][:, :], r_buf[:, s, :], ACT.Copy,
                                         bias=at0, scale=slope).then_inc(lines_done, 1)
                if not first:
                    high_part(i, j, j - 1)
                nc.scalar.activation(line["P3"][:, :], r_buf[:, s, :], ACT.Copy,
                                     bias=LINE_P3[1], scale=LINE_P3[0]).then_inc(lines_done, 1)

            def high_part(i, j, jp):
                act.wait_ge(combos_done, 8 * (number(i, jp) + 1))
                inner = jp < 0 and not (isinstance(i, int) and i == 0)
                mat, mt, half, _ = half_at(NBODY + jp if inner else jp)
                if inner or (jp >= 10):
                    act.wait_ge(up_ready, PAIRS * i if inner else PAIRS * i + PAIRS)
                elif jp in (6, 7, 8, 9):
                    act.wait_ge(up_ready, PAIRS * i + CT)
                elif jp in (0, 1) and not (isinstance(i, int) and i == 0):
                    act.wait_ge(up_ready, PAIRS * i)
                elif jp in (2, 3, 4, 5) and not (isinstance(i, int) and i == 0):
                    act.wait_ge(down_ready, ADDS * i)
                elif jp in (-2, -1, 0):
                    act.wait_ge(t2_done, 2 * NJ)
                dst = (down_w[:, mt] if mat == 2 else gu_w[mt][:, mat])
                cols = slice(HALF * half, HALF * half + HALF)
                nc.scalar.activation(dst[:, 0, cols], w_buf[:, :], ACT.Copy, bias=0.0,
                                     scale=1.0).then_inc(his_done, 1)
                if mat == 2:
                    nc.scalar.activation(dst[:, 2, cols], w_buf[:, :], ACT.Copy, bias=0.0,
                                         scale=2.0 ** -11).then_inc(his_done, 1)

            def silu(i, p):
                n = PAIRS * i + p
                act.wait_ge(gate_ready, n + 1)
                if not (isinstance(n, int) and n == 0):
                    act.wait_ge(hlo_done, n)
                nc.scalar.activation(s_buf[:, :], ps[:, p % 2, :], ACT.Silu, bias=0.0,
                                     scale=g_back[:, 0:1]).then_inc(gate_read, 1)

            def h_high(i, p):
                n = PAIRS * i + p
                act.wait_ge(up_read, n + 1)
                if not (isinstance(i, int) and i == 0):
                    act.wait_ge(down_ready, ADDS * i)
                nc.scalar.activation(h_hl[:, p // CT, 0, (p % CT) * TOK:(p % CT + 1) * TOK], s_buf[:, :],
                                     ACT.Copy, bias=0.0, scale=2.0 ** -11).then_inc(hhi_done, 1)

            def root(c):
                act.wait_ge(var_ready, c + 1)
                nc.scalar.activation(std[:, :], var_eps[:, :], ACT.Sqrt, bias=0.0,
                                     scale=1.0).then_inc(std_ready, 1)

            for ct in range(CT):
                root(ct)
                act.wait_ge(ln_ready, ct + 1)
                for n in range(B):
                    nc.scalar.activation(y_nat[ct][:, :, n, :],
                                         acc[:, B * ct + n, :].rearrange("p (b l) -> p b l", l=32), ACT.Identity,
                                         bias=ln_bias[:, ct % 2, n:n + 1],
                                         scale=ln_scale[:, ct % 2, n:n + 1]).then_inc(y_ready, 1)
            unpack_lines(0, -6)

            def copy_yt(ct, g):
                k = LG * ct + g
                act.wait_ge(t_done, k + 1)
                if ct:
                    act.wait_ge(m_done, k - LG + 1)
                nc.scalar.activation(y_t[:, 4 * g:4 * g + 4, :], ps[:, k % 2, :].rearrange("p (b c) -> p b c", c=P),
                                     ACT.Copy, bias=0.0, scale=1.0).then_inc(t_read, 1)

            for g in range(LG // 2):
                copy_yt(0, g)
            act.wait_ge(diff_ready, 1)
            nc.scalar.activation(prob[:, :, :], scores[:, :, :], ACT.Exp, bias=0.0,
                                 scale=float(C) ** -0.5).then_inc(exp_ready, 1)
            for g in range(LG // 2, LG):
                copy_yt(0, g)
            unpack_lines(0, -5)

            def normalise(ct):
                act.wait_ge(ln_ready, CT + ct + 1)
                for n in range(B):
                    for f in range(2):
                        k = 2 * (B * ct + n) + f
                        if k >= 2:
                            act.wait_ge(t2_done, k - 1)
                        nc.scalar.activation(xn_buf[:, f, :], acc[:, B * ct + n, f * 512:f * 512 + 512],
                                             ACT.Identity, bias=ln_bias[:, ct % 2, n:n + 1],
                                             scale=ln_scale[:, ct % 2, n:n + 1]).then_inc(xn_ready, 1)
                        if k >= 1 and not (n == 0 and f == 0):
                            x_high(k - 1)
                x_high(2 * (B * ct + B - 1) + 1)

            def x_high(k):
                j, f = k // 2, k % 2
                ct, n = j // B, j % B
                act.wait_ge(t2_done, k + 1)
                nc.scalar.activation(xn_t[ct][:, 0, 4 * f:4 * f + 4, n * P:n * P + P],
                                     ps[:, 4 + k % 4, :].rearrange("p (k c) -> p k c", c=P),
                                     ACT.Copy, bias=0.0, scale=1.0).then_inc(xhi_done, 1)

            for ct in range(CT):
                if ct + 1 < CT:
                    for g in range(LG):
                        copy_yt(ct + 1, g)
                if ct >= 1:
                    normalise(ct - 1)
                if ct == CT - 1:
                    unpack_lines(0, -4)
                    unpack_lines(0, -3)
                    unpack_lines(0, -2)
                root(CT + ct)
            normalise(CT - 1)
            unpack_lines(0, -1)

            def chunk(i, last=False):
                unpack_lines(i, 0)
                unpack_lines(i, 1)
                for p in range(PAIRS):
                    silu(i, p)
                    if not last or p < NLAST - 2:
                        unpack_lines(i, 2 + p)
                    elif p == NLAST - 2:
                        high_part(i, NLAST, NLAST - 1)
                    h_high(i, p)
                if not last:
                    unpack_lines(i, 10)
                    unpack_lines(i, 11)

            chunk(0)
            with act.Fori(1, NCHUNK - 1) as i:
                chunk(i)
            chunk(NCHUNK - 1, last=True)

        @block.vector
        def _(dve):
            chained = [0]

            def link(ins):
                chained[0] += 1
                ins.then_inc(v_chain, 1)
                dve.wait_ge(v_chain, chained[0])

            def unpack(i, j, step):
                k = number(i, j)
                first = isinstance(k, int) and k == 0
                s = (NA + j) % 2
                v = nc.vector
                if step == 0:
                    dve.wait_ge(lines_done, 8 * k + 4)
                    v.tensor_tensor(line["N1"][:, :], line["N0"][:, :], line["N1"][:, :],
                                    ALU.min).then_inc(combos_done, 1)
                elif step == 1:
                    dve.wait_ge(lines_done, 8 * k + 5)
                    v.scalar_tensor_tensor(out=line["P1"][:, :], in0=line["P0"][:, :], scalar=0.0,
                                           in1=line["P1"][:, :], op0=ALU.max,
                                           op1=ALU.max).then_inc(combos_done, 1)
                elif step == 2:
                    dve.wait_ge(lines_done, 8 * k + 7)
                    dve.wait_ge(combos_done, 8 * k + 1)
                    v.tensor_tensor(line["N2"][:, :], line["N1"][:, :], line["N2"][:, :],
                                    ALU.min).then_inc(combos_done, 1)
                elif step == 3:
                    dve.wait_ge(combos_done, 8 * k + 2)
                    v.tensor_tensor(line["P2"][:, :], line["P1"][:, :], line["P2"][:, :],
                                    ALU.max).then_inc(combos_done, 1)
                elif step == 4:
                    dve.wait_ge(combos_done, 8 * k + 3)
                    v.scalar_tensor_tensor(out=line["N2"][:, :], in0=r_buf[:, s, :], scalar=SLOPE_67,
                                           in1=line["N2"][:, :], op0=ALU.mult,
                                           op1=ALU.min).then_inc(combos_done, 1)
                elif step == 5:
                    dve.wait_ge(lines_done, 8 * k + 8)
                    dve.wait_ge(combos_done, 8 * k + 4)
                    v.tensor_tensor(line["P3"][:, :], line["P2"][:, :], line["P3"][:, :],
                                    ALU.max).then_inc(combos_done, 1)
                elif step == 6:
                    if not first:
                        low_part(i, j - 1)
                elif step == 7:
                    dve.wait_ge(combos_done, 8 * k + 6)
                    v.scalar_tensor_tensor(out=line["P3"][:, :], in0=line["N2"][:, :], scalar=0.0,
                                           in1=line["P3"][:, :], op0=ALU.min,
                                           op1=ALU.add).then_inc(combos_done, 1)
                else:
                    mat = half_at(j)[0]
                    dve.wait_ge(a_arrived[s], 16 * ((NBODY // 2) * i + (NA + j) // 2 + 1))
                    dve.wait_ge(combos_done, 8 * k + 7)
                    if not first:
                        dve.wait_ge(los_done, k)
                    v.scalar_tensor_tensor(out=w_buf[:, :], in0=line["P3"][:, :],
                                           scalar=w_scale[:, mat:mat + 1], in1=a_in[:, s, :],
                                           op0=ALU.mult, op1=ALU.mult).then_inc(combos_done, 1)

            def low_part(i, jp):
                inner = jp < 0 and not (isinstance(i, int) and i == 0)
                mat, mt, half, _ = half_at(NBODY + jp if inner else jp)
                dst = (down_w[:, mt] if mat == 2 else gu_w[mt][:, mat])
                cols = slice(HALF * half, HALF * half + HALF)
                dve.wait_ge(his_done, his_until(i - 1, NBODY + jp) if inner else his_until(i, jp))
                nc.vector.tensor_tensor(dst[:, 1, cols], w_buf[:, :], dst[:, 0, cols],
                                        ALU.subtract).then_inc(los_done, 1)

            def unpack_half(i, j):
                for step in range(9):
                    unpack(i, j, step)

            def h_product(i, p):
                n = PAIRS * i + p
                dve.wait_ge(up_ready, n + 1)
                dve.wait_ge(gate_read, n + 1)
                nc.vector.scalar_tensor_tensor(out=s_buf[:, :], in0=ps[:, 2 + p % 2, :],
                                               scalar=u_back[:, 0:1], in1=s_buf[:, :],
                                               op0=ALU.mult, op1=ALU.mult).then_inc(up_read, 1)

            def h_low(i, p):
                n = PAIRS * i + p
                dst = h_hl[:, p // CT, :, (p % CT) * TOK:(p % CT + 1) * TOK]
                dve.wait_ge(hhi_done, n + 1)
                nc.vector.scalar_tensor_tensor(out=dst[:, 1, :], in0=dst[:, 0, :], scalar=-2048.0,
                                               in1=s_buf[:, :], op0=ALU.mult,
                                               op1=ALU.add).then_inc(hlo_done, 1)

            def add(i, a):
                t, f = a // 2, a % 2
                n = ADDS * i + a
                dve.wait_ge(down_ready, n + 1)
                if not (isinstance(i, int) and i == 0):
                    dve.wait_ge(down_added, n - ADDS + 1)
                cols = slice(512 * f, 512 * f + 512)
                nc.vector.scalar_tensor_tensor(out=acc[:, t, cols], in0=ps[:, 4 + a % 4, :],
                                               scalar=y_back[:, 0:1], in1=acc[:, t, cols],
                                               op0=ALU.mult, op1=ALU.add).then_inc(down_added, 1)

            def norm_stats(c, ct, gain):
                v = nc.vector
                for n in range(B):
                    j = B * ct + n
                    if c < CT:
                        dve.wait_ge(x_in[j], 16)
                    v.bn_stats(stats[:, n, 0, :], acc[:, j, 0:512]).then_inc(v_chain, 1)
                    v.bn_stats(stats[:, n, 1, :], acc[:, j, 512:1024]).then_inc(v_chain, 1)
                    chained[0] += 2
                dve.wait_ge(v_chain, chained[0])
                for n in range(B):
                    v.bn_aggr(mean_var[:, n, :], stats[:, n, :, :].rearrange("p a b -> p (a b)")).then_inc(v_chain, 1)
                    chained[0] += 1
                dve.wait_ge(v_chain, chained[0])
                v.tensor_scalar(var_eps[:, :], mean_var[:, :, 1], 1e-5, None, ALU.add).then_inc(var_ready, 1)
                dve.wait_ge(std_ready, c + 1)
                link(v.reciprocal(rstd[:, :], std[:, :]))
                link(v.tensor_tensor(tmp4[:, :], rstd[:, :], rstd[:, :], ALU.mult))
                link(v.tensor_tensor(tmp4[:, :], tmp4[:, :], var_eps[:, :], ALU.mult))
                link(v.tensor_scalar(tmp4[:, :], tmp4[:, :], -0.5 * gain, 1.5 * gain, ALU.mult, ALU.add))
                if c >= 2 and c < CT:
                    dve.wait_ge(y_ready, B * (c - 1))
                elif c >= CT + 2:
                    dve.wait_ge(xn_ready, 2 * B * (c - CT - 1))
                link(v.tensor_tensor(ln_scale[:, ct % 2, :], tmp4[:, :], rstd[:, :], ALU.mult))
                v.scalar_tensor_tensor(out=ln_bias[:, ct % 2, :], in0=mean_var[:, :, 0], scalar=-1.0,
                                       in1=ln_scale[:, ct % 2, :], op0=ALU.mult,
                                       op1=ALU.mult).then_inc(ln_ready, 1)

            v = nc.vector
            norm_stats(0, 0, 1.0)
            dve.wait_ge(absmax_in, 16)
            v.tensor_reduce(amax[:, :], absmax_sb, AX, ALU.max, apply_absolute_value=True).then_inc(amax_sem, 1)
            norm_stats(1, 1, 1.0)
            dve.wait_ge(amax_red, 1)
            link(v.tensor_scalar(amax[:, :], amax_all[:, :], 2.0 ** -30, 2.0 ** 30, ALU.max, ALU.min))
            link(v.tensor_scalar(pow2[:, :].bitcast(I32), amax[:, :].bitcast(I32), 0x7F800000, None,
                                 ALU.bitwise_and))
            link(v.reciprocal(w_scale[:, :], pow2[:, :]))
            link(v.tensor_scalar(u_back[:, :], w_scale[:, 0:1], 2.0 ** -20, None, ALU.mult))
            link(v.tensor_scalar(w_scale[:, :], w_scale[:, :], 2.0 ** 14, None, ALU.mult))
            link(v.tensor_scalar(g_back[:, :], pow2[:, 0:1], 2.0 ** -24, None, ALU.mult))
            link(v.scalar_tensor_tensor(out=y_back[:, :], in0=pow2[:, 0:1], scalar=2.0 ** -7,
                                        in1=pow2[:, 1:2], op0=ALU.mult, op1=ALU.mult))
            link(v.tensor_tensor(y_back[:, :], y_back[:, :], pow2[:, 2:3], ALU.mult))
            norm_stats(2, 2, 1.0)
            norm_stats(3, 3, 1.0)
            unpack_half(0, -6)

            dve.wait_ge(consts, 12)
            dve.wait_ge(gram_done, CT)
            half_lb = LB // 2
            for f in range(2):
                rows = slice(half_lb * B * f, half_lb * B * (f + 1))
                v.tensor_tensor(masked[:, rows, :], gram[:, half_lb * f:half_lb * (f + 1), :, :]
                                .rearrange("p b m l -> p (b m) l"),
                                mask32[:, None, :].broadcast_to([P, half_lb * B, 32]),
                                ALU.mult).then_inc(gram_read, 1)
                dve.wait_ge(gram_read, f + 1)
                link(v.tensor_reduce(scores[:, half_lb * f:half_lb * (f + 1), :]
                                     .rearrange("p b m -> p (b m)"), masked[:, rows, :], AX, ALU.add))
            link(v.tensor_reduce(row_stat[:, :], scores[:, :, :], AX, ALU.max))
            v.tensor_tensor(scores[:, :, :], scores[:, :, :],
                            row_stat[:, :, None].broadcast_to([P, LB, B]), ALU.subtract).then_inc(diff_ready, 1)
            dve.wait_ge(exp_ready, 1)
            link(v.tensor_reduce(row_stat[:, :], prob[:, :, :], AX, ALU.add))
            link(v.reciprocal(row_stat[:, :], row_stat[:, :]))
            v.tensor_tensor(prob[:, :, :], prob[:, :, :],
                            row_stat[:, :, None].broadcast_to([P, LB, B]), ALU.mult).then_inc(prob_ready, 1)
            dve.wait_ge(rep_done, 1)
            for m in range(B):
                rows = slice(32 * m, 32 * m + 32)
                v.tensor_tensor(prob_m[rows, :, :],
                                ps[rows, 4, :].rearrange("p (n b m) -> p b n m", n=B, m=B)[:, :, :, m],
                                same_n[rows, None, :].broadcast_to([32, LB, B]), ALU.add).then_inc(v_chain, 1)
                chained[0] += 1
            dve.wait_ge(v_chain, chained[0])
            for f in range(2):
                rows = slice(half_lb * f, half_lb * (f + 1))
                v.tensor_tensor(d_mat[:, rows, :, :].rearrange("p b n l -> p (b n) l"),
                                prob_m[:, rows, :].rearrange("p b n -> p (b n)")[:, :, None]
                                .broadcast_to([P, half_lb * B, 32]),
                                mask32[:, None, :].broadcast_to([P, half_lb * B, 32]),
                                ALU.mult).then_inc(d_ready, 1)
            unpack_half(0, -5)

            def add_messages(ct):
                for g in range(LG):
                    k = LG * ct + g
                    dve.wait_ge(m_done, k + 1)
                    dst = acc[:, B * ct:B * ct + B, P * g:P * g + P]
                    v.tensor_tensor(dst, ps[:, 2 + k % 2, :].rearrange("p (n l) -> p n l", n=B), dst,
                                    ALU.add).then_inc(x1_ready, 1)
                dve.wait_ge(x1_ready, LG * ct + LG)

            def x_lows(ct):
                for k in range(2 * B * ct, 2 * B * (ct + 1)):
                    j, f = k // 2, k % 2
                    dst = xn_t[ct][:, :, 4 * f:4 * f + 4, (j % B) * P:(j % B) * P + P]
                    dve.wait_ge(xhi_done, k + 1)
                    v.tensor_tensor(dst[:, 1], ps[:, 4 + k % 4, :].rearrange("p (k c) -> p k c", c=P),
                                    dst[:, 0], ALU.subtract).then_inc(xlo_done, 1)

            for ct in range(CT):
                add_messages(ct)
                if ct >= 1:
                    x_lows(ct - 1)
                if ct == CT - 1:
                    unpack_half(0, -4)
                    unpack_half(0, -3)
                    unpack_half(0, -2)
                norm_stats(CT + ct, ct, 1024.0)
            x_lows(CT - 1)
            unpack_half(0, -1)

            def chunk(i, last=False):
                unpack_half(i, 0)
                unpack_half(i, 1)
                for p in range(PAIRS):
                    h_product(i, p)
                    if not last or p < NLAST - 2:
                        unpack_half(i, 2 + p)
                    elif p == NLAST - 2:
                        low_part(i, NLAST - 1)
                    h_low(i, p)
                done = 0
                for a in range(ADDS):
                    add(i, a)
                    if not last:
                        while done < (a + 1) * 18 // ADDS:
                            unpack(i, 10 + done // 9, done % 9)
                            done += 1

            chunk(0)
            with dve.Fori(1, NCHUNK - 1) as i:
                chunk(i)
            chunk(NCHUNK - 1, last=True)

        @block.tensor
        def _(pe):
            mm = nc.tensor.matmul
            for ct in range(CT):
                pe.wait_ge(y_ready, B * (ct + 1))
                if ct == 0:
                    pe.wait_ge(consts, 12)
                for lb in range(LB):
                    cols = y_nat[ct][:, lb, :, :].rearrange("p n l -> p (n l)")
                    last = mm(gram[:, lb, :, :], cols, cols, start=(ct == 0 and lb % 4 == 0),
                              stop=(ct == CT - 1), skip_group_check=True)
                last.then_inc(gram_done, 1)

            def transpose_y(ct, g):
                k = LG * ct + g
                if k == 0:
                    pe.wait_ge(gram_read, 1)
                elif k >= 2:
                    pe.wait_ge(t_read, k - 1)
                for b in range(4):
                    lb = 4 * g + b
                    last = nc.tensor.transpose(ps[:, k % 2, P * b:P * b + P],
                                               y_nat[ct][:, lb, :, :].rearrange("p n l -> p (n l)"), ident[:, :])
                last.then_inc(t_done, 1)

            def messages(ct, g):
                k = LG * ct + g
                pe.wait_ge(t_read, k + 1)
                if ct == 0:
                    pe.wait_ge(d_ready, 1 + g // (LG // 2))
                if k >= 2:
                    pe.wait_ge(x1_ready, k - 1)
                bank = ps[:, 2 + k % 2, :].rearrange("p (n b l) -> p n b l", n=B, l=32)
                for b in range(4):
                    lb = 4 * g + b
                    last = mm(bank[:, :, b, :], y_t[:, lb, :], d_mat[:, lb, :, :], start=True, stop=True)
                last.then_inc(m_done, 1)

            def transpose_xn(ct):
                for k in range(2 * B * ct, 2 * B * (ct + 1)):
                    pe.wait_ge(xn_ready, k + 1)
                    if k >= 4:
                        pe.wait_ge(xlo_done, k - 3)
                    for b in range(4):
                        last = nc.tensor.transpose(ps[:, 4 + k % 4, P * b:P * b + P],
                                                   xn_buf[:, k % 2, P * b:P * b + P], ident[:, :])
                    last.then_inc(t2_done, 1)

            def gate_up(i, p):
                n = PAIRS * i + p
                mt, ct = p // CT, p % CT
                for g, bank, ready, read in ((0, p % 2, gate_ready, gate_read), (1, 2 + p % 2, up_ready, up_read)):
                    if ct == 0:
                        pe.wait_ge(los_done, NBODY * i + 4 * mt + 2 * g + 2)
                    if not (isinstance(n, int) and n < 2):
                        pe.wait_ge(read, n - 1)
                    w = gu_w[mt][:, g]
                    for kt in range(KT):
                        hi, lo = w[:, 0, P * kt:P * kt + P], w[:, 1, P * kt:P * kt + P]
                        mm(ps[:, bank, :], hi, xn_t[ct][:, 0, kt, :], start=(kt == 0), stop=False)
                        mm(ps[:, bank, :], hi, xn_t[ct][:, 1, kt, :], start=False, stop=False)
                        last = mm(ps[:, bank, :], lo, xn_t[ct][:, 0, kt, :], start=False, stop=(kt == KT - 1))
                    last.then_inc(ready, 1)

            def down(i, t):
                if t == 0:
                    pe.wait_ge(los_done, NBODY * i + NA + 6)
                if t % B == 0:
                    pe.wait_ge(hlo_done, PAIRS * i + PAIRS - CT + t // B + 1)
                for f in range(2):
                    a = 2 * t + f
                    n = ADDS * i + a
                    if not (isinstance(n, int) and n < 4):
                        pe.wait_ge(down_added, n - 3)
                for mt in range(CM):
                    for part, sides in ((0, (0, 1)), (1, (2,))):
                        for s in sides:
                            for f in range(2):
                                a = 2 * t + f
                                last = mm(ps[:, 4 + a % 4, :], h_hl[:, mt, part, P * t:P * t + P],
                                          down_w[:, mt, s, 512 * f:512 * f + 512],
                                          start=(mt == 0 and part == 0 and s == 0),
                                          stop=(mt == CM - 1 and part == 1))
                                if mt == CM - 1 and part == 1:
                                    last.then_inc(down_ready, 1)

            for g in range(LG):
                transpose_y(0, g)
            pe.wait_ge(prob_ready, 1)
            pe.wait_ge(gram_read, 2)
            for n in range(B):
                last = mm(ps[:, 4, P * n:P * n + P], rep[:, n, :], prob[:, :, :], start=True, stop=True)
            last.then_inc(rep_done, 1)
            for ct in range(CT):
                for g in range(LG):
                    messages(ct, g)
                    if ct + 1 < CT:
                        transpose_y(ct + 1, g)
                if 1 <= ct < CT - 1:
                    transpose_xn(ct - 1)
            transpose_xn(CT - 2)
            pe.wait_ge(xlo_done, 2 * B)
            gate_up(0, 0)
            transpose_xn(CT - 1)
            for i, p in ((0, p) for p in range(1, PAIRS)):
                if p < CT:
                    pe.wait_ge(xlo_done, 2 * B * (p + 1))
                gate_up(i, p)
            for t in range(NJ):
                down(0, t)
            with pe.Fori(1, NCHUNK - 1) as i:
                for p in range(PAIRS):
                    gate_up(i, p)
                for t in range(NJ):
                    down(i, t)
            for p in range(PAIRS):
                gate_up(NCHUNK - 1, p)
            for t in range(NJ):
                down(NCHUNK - 1, t)


def stream_order():
    for mat, mt, half, _ in AHEAD:
        yield mat, mt, half
    for i in range(NCHUNK):
        for mat, mt, half, nxt in (BODY if i < NCHUNK - 1 else BODY[:NLAST]):
            yield mat, CM * (i + nxt) + mt, half


def kernel(L0_attn_x, L0_ffn_gate_q, L0_ffn_gate_absmax, L0_ffn_up_q, L0_ffn_up_absmax,
           L0_ffn_down_q, L0_ffn_down_absmax):
    import numpy as np
    import concourse.bacc as bacc
    from concourse.bass_utils import run_bass_kernel_spmd

    x = np.ascontiguousarray(L0_attn_x)
    q = [np.asarray(L0_ffn_gate_q), np.asarray(L0_ffn_up_q), np.asarray(L0_ffn_down_q)]
    a = [np.asarray(v) for v in (L0_ffn_gate_absmax, L0_ffn_up_absmax, L0_ffn_down_absmax)]
    absmax = np.stack(a)
    q_half, a_half = [], []
    for mat in (0, 1):
        q_half.append(q[mat].reshape(M // P, P, 2, KT // 2, P).transpose(0, 2, 4, 3, 1)
                      .reshape(M // P, 2, P, HALF))
        a_half.append(a[mat].reshape(M // P, P, 2, KT // 2, 2).transpose(0, 2, 4, 3, 1)
                      .reshape(M // P, 2, 2, HALF))
    q_half.append(q[2].reshape(2, HALF, M // P, P).transpose(2, 0, 3, 1))
    a_half.append(a[2].reshape(2, HALF, M // P, 2).transpose(2, 0, 3, 1))
    order = list(stream_order())
    q_stream = np.stack([q_half[mat][mt, half] for mat, mt, half in order])
    a_stream = np.stack([a_half[mat][mt, half] for mat, mt, half in order])

    nc = bacc.Bacc("TRN2", target_bir_lowering=False, num_devices=1)
    arrays = {"x_dram": x, "q_dram": q_stream, "a_dram": a_stream, "absmax_dram": absmax}
    args = [nc.dram_tensor(n, v.shape, mybir.dt.from_np(v.dtype), kind="ExternalInput").ap()
            for n, v in arrays.items()]
    args.append(nc.dram_tensor("out_dram", x.shape, mybir.dt.from_np(x.dtype), kind="ExternalOutput").ap())
    block_kernel(nc, *args)
    return run_bass_kernel_spmd(nc, [arrays], core_ids=[0]).results[0]["out_dram"]
```

```python
import concourse.bass as bass
from concourse import mybir
from contextlib import ExitStack

P = 128
B, C, L = 4, 512, 1024
M = 3584
BLOCK = 64
CT = C // P
TOK = B * P
NJ = CT * B
KT = L // P
LB = L // 32
LG = LB // 4
CM = 2
NCHUNK = M // P // CM
HALF = 512
PAIRS = CM * CT
ADDS = NJ * 2

AHEAD = [(0, 0, 0, 0), (0, 0, 1, 0), (1, 0, 0, 0), (1, 0, 1, 0), (0, 1, 0, 0), (0, 1, 1, 0)]
BODY = [(1, 1, 0, 0), (1, 1, 1, 0),
        (2, 0, 0, 0), (2, 0, 1, 0), (2, 1, 0, 0), (2, 1, 1, 0),
        (0, 0, 0, 1), (0, 0, 1, 1), (1, 0, 0, 1), (1, 0, 1, 1),
        (0, 1, 0, 1), (0, 1, 1, 1)]
NA = len(AHEAD)
NBODY = len(BODY)
NLAST = 6
WITH_PAIR = [(2,), (3,), (4,), (5,), (6, 7), (8,), (9,), ()]
WITH_PAIR_FIRST = [(0,), (1,), (2,), (3, 4), (5, 6), (7, 8), (9,), ()]
LINES_FIRST = 5
NHALVES = NA + NBODY * (NCHUNK - 1) + NLAST

LINE_N0 = (0.30380716919898987, 1.1266502141952515)
LINE_N1 = (0.13015556335449219, 0.12570476531982422)
LINE_N2 = (0.09966795146465302, 0.014562472701072693)
SLOPE_67 = 0.09105003625154495
LINE_P0 = (0.08134990185499191, -0.001769602298736572)
LINE_P1 = (0.0918029397726059, -0.029296517372131348)
LINE_P2 = (0.1219071745872498, -0.16882604360580444)
LINE_P3 = (0.2770431637763977, -1.2163453102111816)


def half_at(j):
    return AHEAD[NA + j] if j < 0 else BODY[j]


def n_his(j):
    return 2 if half_at(j)[0] == 2 else 1


HIS_AHEAD = sum(n_his(j) for j in range(-NA, 0))
HIS_BODY = sum(n_his(j) for j in range(NBODY))


def his_until(i, j):
    if j < 0:
        return sum(n_his(t) for t in range(-NA, j + 1))
    return HIS_BODY * i + HIS_AHEAD + sum(n_his(t) for t in range(j + 1))


def number(i, j):
    return NBODY * i + NA + j


def block_kernel(nc: bass.Bass, x, q_stream, a_stream, absmax, out):
    F32, F16, I32 = mybir.dt.float32, mybir.dt.float16, mybir.dt.int32
    ALU = mybir.AluOpType
    ACT = mybir.ActivationFunctionType
    AX = mybir.AxisListType.X

    ctx = ExitStack()
    with ctx:
        def sb(name, shape, dt):
            return ctx.enter_context(nc.sbuf_tensor(name, shape, dt))

        def sem(name):
            return ctx.enter_context(nc.semaphore(name))

        acc = sb("acc", [P, NJ, L], F32)
        blk = sb("blk", [P, CT, B * L], F32)
        h_mem = sb("h_mem", [P, 4096], F32)
        w_mem = sb("w_mem", [P, 3 * 1024 + 2048 + 2048], F32)
        h_hl = h_mem[:, :].bitcast(F16).rearrange("p (m s t) -> p m s t", m=CM, s=2)
        down_w = w_mem[:, 0:3072].bitcast(F16).rearrange("p (m s t) -> p m s t", m=CM, s=3)
        gu_w = [w_mem[:, 5120:7168].bitcast(F16).rearrange("p (g s t) -> p g s t", g=2, s=2),
                w_mem[:, 3072:5120].bitcast(F16).rearrange("p (g s t) -> p g s t", g=2, s=2)]

        q_in = sb("q_in", [P, 2, HALF], I32)
        a_in = sb("a_in", [P, 2, HALF], F32)
        r_buf = sb("r_buf", [P, 2, HALF], F32)
        line = {n: sb(f"line_{n}", [P, HALF], F32) for n in ("N0", "N1", "N2", "P0", "P1", "P2", "P3")}
        w_buf = sb("w_buf", [P, HALF], F32)
        s_buf = sb("s_buf", [P, TOK], F32)

        absmax_sb = h_mem[:, 0:3 * 448].rearrange("p (a b) -> p a b", a=3)
        masked = h_mem[:, :].rearrange("p (g l) -> p g l", l=32)
        d_mat = h_mem[:, :].rearrange("p (b n l) -> p b n l", n=B, l=32)
        y_t = w_mem[:, 0:4096].rearrange("p (b c) -> p b c", c=P)
        xn_buf = w_mem[:, 4096:5120].rearrange("p (s t) -> p s t", s=2)
        rep = w_mem[:, 4096:4608].rearrange("p (n m) -> p n m", n=B)
        y_nat = [blk[:, ct, :].rearrange("p (b n l) -> p b n l", n=B, l=32) for ct in range(CT)]
        xn_t = [blk[:, ct, :].bitcast(F16).rearrange("p (s k t) -> p s k t", s=2, k=KT) for ct in range(CT)]

        ident = sb("ident", [P, P], F32)
        mask32 = sb("mask32", [P, 32], F32)
        same_n = sb("same_n", [P, B], F32)
        stats = sb("stats", [P, B, 2, 6], F32)
        mean_var = sb("mean_var", [P, 2, B, 2], F32)
        var_eps = sb("var_eps", [P, B], F32)
        minus_half = sb("minus_half", [P, B], F32)
        ln_scale = sb("ln_scale", [P, 2, B], F32)
        ln_bias = sb("ln_bias", [P, 2, B], F32)
        scores = sb("scores", [P, LB, B], F32)
        row_stat = sb("row_stat", [P, LB], F32)
        prob = sb("prob", [P, LB, B], F32)
        prob_m = sb("prob_m", [P, LB, B], F32)
        amax = sb("amax", [P, 3], F32)
        amax_all = sb("amax_all", [P, 3], F32)
        pow2 = sb("pow2", [P, 3], F32)
        w_scale = sb("w_scale", [P, 3], F32)
        g_back = sb("g_back", [P, 1], F32)
        u_back = sb("u_back", [P, 1], F32)
        y_back = sb("y_back", [P, 1], F32)

        ps = ctx.enter_context(nc.psum_tensor("ps", [P, 8, 512], F32))
        gram = ps[:, :, :].rearrange("p k (b m l) -> p (k b) m l", m=B, l=32)

        absmax_in = sem("absmax_in")
        x_in = [sem(f"x_in{j}") for j in range(NJ)]
        q_arrived = [sem(f"q_arrived{s}") for s in range(2)]
        a_arrived = [sem(f"a_arrived{s}") for s in range(2)]
        out_done = sem("out_done")
        consts = sem("consts")
        amax_sem = sem("amax_sem")
        amax_red = sem("amax_red")
        v_chain = sem("v_chain")
        stats_ready = sem("stats_ready")
        p_chain = sem("p_chain")
        ln_ready = sem("ln_ready")
        y_act = sem("y_act")
        y_pool = sem("y_pool")
        y_dve = sem("y_dve")
        gram_done = sem("gram_done")
        gram_read = sem("gram_read")
        diff_ready = sem("diff_ready")
        exp_ready = sem("exp_ready")
        prob_ready = sem("prob_ready")
        rep_done = sem("rep_done")
        d_ready = sem("d_ready")
        t_done = sem("t_done")
        t_read = sem("t_read")
        m_done = sem("m_done")
        x1_ready = sem("x1_ready")
        xn_ready = sem("xn_ready")
        t2_done = sem("t2_done")
        xhi_done = sem("xhi_done")
        xlo_done = sem("xlo_done")
        lines_done = sem("lines_done")
        combos_done = sem("combos_done")
        his_done = sem("his_done")
        los_done = sem("los_done")
        gate_ready = sem("gate_ready")
        up_ready = sem("up_ready")
        gate_read = sem("gate_read")
        up_read = sem("up_read")
        hhi_done = sem("hhi_done")
        hlo_done = sem("hlo_done")
        down_ready = sem("down_ready")
        down_added = sem("down_added")

        x_v = x.rearrange("n (t p) l -> t n p l", p=P)
        out_v = out.rearrange("n (t p) l -> t n p l", p=P)
        block = ctx.enter_context(nc.Block())

        @block.sync
        def _(sp):
            def load_half(k, s, wait=None):
                if wait is not None:
                    sp.wait_ge(lines_done, 8 * (wait) + 1)
                sp.dma_start(q_in[:, s, :], q_stream[k, :, :]).then_inc(q_arrived[s], 16)
                if wait is not None:
                    sp.wait_ge(combos_done, 8 * (wait) + 8)
                sp.dma_start(a_in[:, s, :],
                             a_stream[k, :, :].rearrange("(o t) n -> o t n", o=2)
                             .broadcast_to([2, BLOCK, HALF])).then_inc(a_arrived[s], 16)

            for j in range(NJ):
                sp.dma_start(acc[:, j, :], x_v[j // B, j % B]).then_inc(x_in[j], 16)
            sp.dma_start(absmax_sb, absmax.rearrange("a (p b) -> p a b", p=P)).then_inc(absmax_in, 16)
            for k in range(2):
                load_half(k, k)
            for k in range(2, NA):
                load_half(k, k % 2, k - 2)
            with sp.Fori(0, NCHUNK - 1) as i:
                for j in range(NBODY):
                    load_half(NBODY * i + NA + j, j % 2, NBODY * i + NA + j - 2)
            for j in range(NLAST):
                k = number(NCHUNK - 1, j)
                load_half(k, k % 2, k - 2)
            for j in range(NJ):
                sp.wait_ge(down_added, ADDS * (NCHUNK - 1) + 2 * j + 2)
                sp.dma_start(out_v[j // B, j % B], acc[:, j, :]).then_inc(out_done, 16)
            sp.wait_ge(out_done, 16 * NJ)

        @block.gpsimd
        def _(pool):
            nc.gpsimd.memset(ident[:, :], 0.0).then_inc(consts, 1)
            nc.gpsimd.memset(mask32[:, :], 0.0).then_inc(consts, 1)
            nc.gpsimd.memset(rep, 0.0).then_inc(consts, 1)
            nc.gpsimd.memset(same_n[:, :], 1.0).then_inc(consts, 1)
            pool.wait_ge(consts, 4)
            nc.gpsimd.affine_select(out=ident[:, :], in_=ident[:, :], compare_op=ALU.not_equal, fill=1.0,
                                    base=0, pattern=[[-1, P]], channel_multiplier=1).then_inc(consts, 1)
            for a in range(4):
                pool.wait_ge(consts, 5 + a)
                nc.gpsimd.affine_select(out=mask32[:, :], in_=mask32[:, :], compare_op=ALU.not_equal,
                                        fill=1.0, base=-32 * a, pattern=[[-1, 32]],
                                        channel_multiplier=1).then_inc(consts, 1)
            rep4 = rep.rearrange("p n (m l) -> p n m l", l=32)
            nc.gpsimd.affine_select(out=rep4, in_=rep4, compare_op=ALU.not_equal, fill=1.0, base=0,
                                    pattern=[[-32, B], [0, 4], [-1, 32]],
                                    channel_multiplier=1).then_inc(consts, 1)
            nc.gpsimd.affine_select(out=same_n[:, :], in_=same_n[:, :], compare_op=ALU.is_ge, fill=0.0,
                                    base=0, pattern=[[-32, B]], channel_multiplier=1).then_inc(consts, 1)
            pool.wait_ge(consts, 11)
            nc.gpsimd.affine_select(out=same_n[:, :], in_=same_n[:, :], compare_op=ALU.is_ge, fill=0.0,
                                    base=31, pattern=[[32, B]], channel_multiplier=-1).then_inc(consts, 1)
            nc.gpsimd.memset(minus_half[:, :], -0.5).then_inc(consts, 1)
            pool.wait_ge(consts, 13)

            chained = [0]

            def link(ins):
                chained[0] += 1
                ins.then_inc(p_chain, 1)
                pool.wait_ge(p_chain, chained[0])

            def norm_factors(c, gain):
                g, s = nc.gpsimd, c % 2
                pool.wait_ge(stats_ready, B * (c + 1))
                if c in (2, 3):
                    pool.wait_ge(y_act, 2 * (c - 1))
                    pool.wait_ge(y_dve, c - 1)
                elif c >= 4:
                    pool.wait_ge(y_act, 2 * CT)
                    pool.wait_ge(y_dve, CT)
                link(g.tensor_scalar(var_eps[:, :], mean_var[:, s, :, 1], 1e-5, None, ALU.add))
                link(g.tensor_tensor(ln_scale[:, s, :], var_eps[:, :], minus_half[:, :], ALU.pow))
                if gain != 1.0:
                    link(g.tensor_scalar(ln_scale[:, s, :], ln_scale[:, s, :], gain, None, ALU.mult))
                link(g.tensor_tensor(ln_bias[:, s, :], mean_var[:, s, :, 0], ln_scale[:, s, :], ALU.mult))
                g.tensor_scalar(ln_bias[:, s, :], ln_bias[:, s, :], -1.0, None, ALU.mult).then_inc(ln_ready, 1)
                pool.wait_ge(ln_ready, c + 1)

            for ct in range(CT):
                norm_factors(ct, 1.0)
                nc.gpsimd.tensor_scalar(y_nat[ct][:, :, 2, :], acc[:, B * ct + 2, :].rearrange("p (b l) -> p b l", l=32),
                                        ln_scale[:, ct % 2, 2:3], ln_bias[:, ct % 2, 2:3],
                                        ALU.mult, ALU.add).then_inc(y_pool, 1)
            pool.wait_ge(amax_sem, 1)
            nc.gpsimd.partition_all_reduce(amax_all[:, :], amax[:, :], P,
                                           bass.bass_isa.ReduceOp.max).then_inc(amax_red, 1)
            for ct in range(CT):
                norm_factors(CT + ct, 1024.0)
                for k in range(2 * B * ct, 2 * B * (ct + 1)):
                    j, f, n = k // 2, k % 2, (k // 2) % B
                    if k >= 2:
                        pool.wait_ge(t2_done, k - 1)
                    nc.gpsimd.tensor_scalar(xn_buf[:, f, :], acc[:, j, f * 512:f * 512 + 512],
                                            ln_scale[:, ct % 2, n:n + 1], ln_bias[:, ct % 2, n:n + 1],
                                            ALU.mult, ALU.add).then_inc(xn_ready, 1)

        @block.scalar
        def _(act):
            def lines_early(i, j):
                k = number(i, j)
                s = (NA + j) % 2
                act.wait_ge(q_arrived[s], 16 * ((NBODY // 2) * i + (NA + j) // 2 + 1))
                if not (isinstance(k, int) and k < 2):
                    act.wait_ge(combos_done, 8 * k - 11)
                nc.scalar.activation(r_buf[:, s, :], q_in[:, s, :], ACT.Copy,
                                     bias=-7.0, scale=1.0).then_inc(lines_done, 1)
                act.wait_ge(lines_done, 8 * k + 1)
                for name, (slope, at0), used in (("N0", LINE_N0, 1), ("P0", LINE_P0, 2),
                                                 ("N1", LINE_N1, 3), ("P1", LINE_P1, 4)):
                    a_line(k, s, name, slope, at0, used)

            def a_line(k, s, name, slope, at0, used):
                if not (isinstance(k, int) and k == 0):
                    act.wait_ge(combos_done, 8 * k - 8 + used)
                nc.scalar.activation(line[name][:, :], r_buf[:, s, :], ACT.Copy,
                                     bias=at0, scale=slope).then_inc(lines_done, 1)

            def lines_late(i, j, high=True):
                k = number(i, j)
                s = (NA + j) % 2
                a_line(k, s, "P2", LINE_P2[0], LINE_P2[1], 6)
                a_line(k, s, "N2", LINE_N2[0], LINE_N2[1], 7)
                if high and not (isinstance(k, int) and k == 0):
                    high_part(i, j, j - 1)
                a_line(k, s, "P3", LINE_P3[0], LINE_P3[1], 8)

            def high_part(i, j, jp):
                act.wait_ge(combos_done, 8 * (number(i, jp) + 1))
                inner = jp < 0 and not (isinstance(i, int) and i == 0)
                mat, mt, half, _ = half_at(NBODY + jp if inner else jp)
                if inner or (jp >= 10):
                    act.wait_ge(up_ready, PAIRS * i if inner else PAIRS * i + PAIRS)
                elif jp in (6, 7, 8, 9):
                    act.wait_ge(up_ready, PAIRS * i + CT)
                elif jp in (0, 1) and not (isinstance(i, int) and i == 0):
                    act.wait_ge(up_ready, PAIRS * i)
                elif jp in (2, 3, 4, 5) and not (isinstance(i, int) and i == 0):
                    act.wait_ge(down_ready, ADDS * i)
                elif jp in (-2, -1, 0):
                    act.wait_ge(t2_done, 2 * NJ)
                dst = (down_w[:, mt] if mat == 2 else gu_w[mt][:, mat])
                cols = slice(HALF * half, HALF * half + HALF)
                nc.scalar.activation(dst[:, 0, cols], w_buf[:, :], ACT.Copy, bias=0.0,
                                     scale=1.0).then_inc(his_done, 1)
                if mat == 2:
                    nc.scalar.activation(dst[:, 2, cols], w_buf[:, :], ACT.Copy, bias=0.0,
                                         scale=2.0 ** -11).then_inc(his_done, 1)

            def silu(i, p):
                n = PAIRS * i + p
                act.wait_ge(gate_ready, n + 1)
                if not (isinstance(n, int) and n == 0):
                    act.wait_ge(hlo_done, n)
                nc.scalar.activation(s_buf[:, :], ps[:, p % 2, :], ACT.Silu, bias=0.0,
                                     scale=g_back[:, 0:1]).then_inc(gate_read, 1)

            def h_high(i, p):
                n = PAIRS * i + p
                act.wait_ge(up_read, n + 1)
                if not (isinstance(i, int) and i == 0):
                    act.wait_ge(down_ready, ADDS * i)
                nc.scalar.activation(h_hl[:, p // CT, 0, (p % CT) * TOK:(p % CT + 1) * TOK], s_buf[:, :],
                                     ACT.Copy, bias=0.0, scale=2.0 ** -11).then_inc(hhi_done, 1)

            for ct in range(CT):
                act.wait_ge(ln_ready, ct + 1)
                for n in range(2):
                    nc.scalar.activation(y_nat[ct][:, :, n, :],
                                         acc[:, B * ct + n, :].rearrange("p (b l) -> p b l", l=32), ACT.Identity,
                                         bias=ln_bias[:, ct % 2, n:n + 1],
                                         scale=ln_scale[:, ct % 2, n:n + 1]).then_inc(y_act, 1)

            def copy_yt(ct, g):
                k = LG * ct + g
                act.wait_ge(t_done, k + 1)
                if ct:
                    act.wait_ge(m_done, k - LG + 1)
                nc.scalar.activation(y_t[:, 4 * g:4 * g + 4, :], ps[:, k % 2, :].rearrange("p (b c) -> p b c", c=P),
                                     ACT.Copy, bias=0.0, scale=1.0).then_inc(t_read, 1)

            def x_highs(ct):
                for k in range(2 * B * ct, 2 * B * (ct + 1)):
                    n, f = (k // 2) % B, k % 2
                    act.wait_ge(t2_done, k + 1)
                    nc.scalar.activation(xn_t[ct][:, 0, 4 * f:4 * f + 4, n * P:n * P + P],
                                         ps[:, 4 + k % 4, :].rearrange("p (k c) -> p k c", c=P),
                                         ACT.Copy, bias=0.0, scale=1.0).then_inc(xhi_done, 1)

            lines_early(0, -6)
            lines_late(0, -6)
            for g in range(4):
                copy_yt(0, g)
            act.wait_ge(diff_ready, 1)
            nc.scalar.activation(prob[:, :, :], scores[:, :, :], ACT.Exp, bias=0.0,
                                 scale=float(C) ** -0.5).then_inc(exp_ready, 1)
            for g in range(4, LG):
                copy_yt(0, g)
            lines_early(0, -5)
            for g in range(LG):
                copy_yt(1, g)
            lines_late(0, -5)
            for ct in (2, 3):
                for g in range(LG):
                    copy_yt(ct, g)
            x_highs(0)
            lines_early(0, -4)
            x_highs(1)
            lines_late(0, -4)
            x_highs(2)
            lines_early(0, -3)
            lines_late(0, -3)
            high_part(0, -2, -3)
            lines_early(0, -2)
            lines_late(0, -2, high=False)
            x_highs(3)
            lines_early(0, -1)
            lines_late(0, -1)

            def chunk(i, with_pair=WITH_PAIR, until=NBODY):
                js = [j for j in range(until)]
                before = [j for j in js if j < with_pair[0][0]]
                lines_early(i, 0)
                for j in before:
                    lines_late(i, j)
                    lines_early(i, j + 1)
                for p in range(PAIRS):
                    silu(i, p)
                    for at, j in enumerate(with_pair[p]):
                        if j < until:
                            lines_late(i, j)
                        elif j == until:
                            high_part(i, j, j - 1)
                        if at == 0:
                            h_high(i, p)
                        if j + 1 < until:
                            lines_early(i, j + 1)
                    if not with_pair[p]:
                        h_high(i, p)
                for j in js:
                    if j > with_pair[-2][-1]:
                        lines_late(i, j)
                        if j + 1 < until:
                            lines_early(i, j + 1)

            chunk(0, WITH_PAIR_FIRST)
            with act.Fori(1, NCHUNK - 1) as i:
                chunk(i)
            chunk(NCHUNK - 1, until=NLAST)

        @block.vector
        def _(dve):
            chained = [0]

            def link(ins):
                chained[0] += 1
                ins.then_inc(v_chain, 1)
                dve.wait_ge(v_chain, chained[0])

            def unpack(i, j, step):
                k = number(i, j)
                first = isinstance(k, int) and k == 0
                s = (NA + j) % 2
                v = nc.vector
                if step == 0:
                    dve.wait_ge(lines_done, 8 * k + 4)
                    v.tensor_tensor(line["N1"][:, :], line["N0"][:, :], line["N1"][:, :],
                                    ALU.min).then_inc(combos_done, 1)
                elif step == 1:
                    dve.wait_ge(lines_done, 8 * k + 5)
                    v.scalar_tensor_tensor(out=line["P1"][:, :], in0=line["P0"][:, :], scalar=0.0,
                                           in1=line["P1"][:, :], op0=ALU.max,
                                           op1=ALU.max).then_inc(combos_done, 1)
                elif step == 2:
                    dve.wait_ge(lines_done, 8 * k + 7)
                    dve.wait_ge(combos_done, 8 * k + 1)
                    v.tensor_tensor(line["N2"][:, :], line["N1"][:, :], line["N2"][:, :],
                                    ALU.min).then_inc(combos_done, 1)
                elif step == 3:
                    dve.wait_ge(combos_done, 8 * k + 2)
                    v.tensor_tensor(line["P2"][:, :], line["P1"][:, :], line["P2"][:, :],
                                    ALU.max).then_inc(combos_done, 1)
                elif step == 4:
                    dve.wait_ge(combos_done, 8 * k + 3)
                    v.scalar_tensor_tensor(out=line["N2"][:, :], in0=r_buf[:, s, :], scalar=SLOPE_67,
                                           in1=line["N2"][:, :], op0=ALU.mult,
                                           op1=ALU.min).then_inc(combos_done, 1)
                elif step == 5:
                    dve.wait_ge(lines_done, 8 * k + 8)
                    dve.wait_ge(combos_done, 8 * k + 4)
                    v.tensor_tensor(line["P3"][:, :], line["P2"][:, :], line["P3"][:, :],
                                    ALU.max).then_inc(combos_done, 1)
                elif step == 6:
                    if not first:
                        low_part(i, j - 1)
                elif step == 7:
                    dve.wait_ge(combos_done, 8 * k + 6)
                    v.scalar_tensor_tensor(out=line["P3"][:, :], in0=line["N2"][:, :], scalar=0.0,
                                           in1=line["P3"][:, :], op0=ALU.min,
                                           op1=ALU.add).then_inc(combos_done, 1)
                else:
                    mat = half_at(j)[0]
                    dve.wait_ge(a_arrived[s], 16 * ((NBODY // 2) * i + (NA + j) // 2 + 1))
                    dve.wait_ge(combos_done, 8 * k + 7)
                    if not first:
                        dve.wait_ge(los_done, k)
                    v.scalar_tensor_tensor(out=w_buf[:, :], in0=line["P3"][:, :],
                                           scalar=w_scale[:, mat:mat + 1], in1=a_in[:, s, :],
                                           op0=ALU.mult, op1=ALU.mult).then_inc(combos_done, 1)

            def low_part(i, jp):
                inner = jp < 0 and not (isinstance(i, int) and i == 0)
                mat, mt, half, _ = half_at(NBODY + jp if inner else jp)
                dst = (down_w[:, mt] if mat == 2 else gu_w[mt][:, mat])
                cols = slice(HALF * half, HALF * half + HALF)
                dve.wait_ge(his_done, his_until(i - 1, NBODY + jp) if inner else his_until(i, jp))
                nc.vector.tensor_tensor(dst[:, 1, cols], w_buf[:, :], dst[:, 0, cols],
                                        ALU.subtract).then_inc(los_done, 1)

            def unpack_half(i, j):
                for step in range(9):
                    unpack(i, j, step)

            def h_product(i, p):
                n = PAIRS * i + p
                dve.wait_ge(up_ready, n + 1)
                dve.wait_ge(gate_read, n + 1)
                nc.vector.scalar_tensor_tensor(out=s_buf[:, :], in0=ps[:, 2 + p % 2, :],
                                               scalar=u_back[:, 0:1], in1=s_buf[:, :],
                                               op0=ALU.mult, op1=ALU.mult).then_inc(up_read, 1)

            def h_low(i, p):
                n = PAIRS * i + p
                dst = h_hl[:, p // CT, :, (p % CT) * TOK:(p % CT + 1) * TOK]
                dve.wait_ge(hhi_done, n + 1)
                nc.vector.scalar_tensor_tensor(out=dst[:, 1, :], in0=dst[:, 0, :], scalar=-2048.0,
                                               in1=s_buf[:, :], op0=ALU.mult,
                                               op1=ALU.add).then_inc(hlo_done, 1)

            def add(i, a):
                t, f = a // 2, a % 2
                n = ADDS * i + a
                dve.wait_ge(down_ready, n + 1)
                if not (isinstance(i, int) and i == 0):
                    dve.wait_ge(down_added, n - ADDS + 1)
                cols = slice(512 * f, 512 * f + 512)
                nc.vector.scalar_tensor_tensor(out=acc[:, t, cols], in0=ps[:, 4 + a % 4, :],
                                               scalar=y_back[:, 0:1], in1=acc[:, t, cols],
                                               op0=ALU.mult, op1=ALU.add).then_inc(down_added, 1)

            def row_stats(c, half):
                n, f = half // 2, half % 2
                j = B * (c % CT) + n
                if c < CT and f == 0:
                    dve.wait_ge(x_in[j], 16)
                nc.vector.bn_stats(stats[:, n, f, :], acc[:, j, 512 * f:512 * f + 512]).then_inc(v_chain, 1)
                chained[0] += 1

            def row_sums(c):
                dve.wait_ge(v_chain, chained[0])
                if c >= 2:
                    dve.wait_ge(ln_ready, c - 1)
                for n in range(B):
                    nc.vector.bn_aggr(mean_var[:, c % 2, n, :],
                                      stats[:, n, :, :].rearrange("p a b -> p (a b)")).then_inc(stats_ready, 1)
                dve.wait_ge(stats_ready, B * (c + 1))

            def y_row(ct):
                dve.wait_ge(ln_ready, ct + 1)
                nc.vector.tensor_scalar(y_nat[ct][:, :, 3, :], acc[:, B * ct + 3, :].rearrange("p (b l) -> p b l", l=32),
                                        ln_scale[:, ct % 2, 3:4], ln_bias[:, ct % 2, 3:4],
                                        ALU.mult, ALU.add).then_inc(y_dve, 1)

            v = nc.vector
            for ct in range(CT):
                for half in range(2 * B):
                    row_stats(ct, half)
                    if half == 3 and ct:
                        y_row(ct - 1)
                row_sums(ct)
            dve.wait_ge(absmax_in, 16)
            v.tensor_reduce(amax[:, :], absmax_sb, AX, ALU.max, apply_absolute_value=True).then_inc(amax_sem, 1)
            y_row(CT - 1)
            dve.wait_ge(amax_red, 1)
            link(v.tensor_scalar(amax[:, :], amax_all[:, :], 2.0 ** -30, 2.0 ** 30, ALU.max, ALU.min))
            link(v.tensor_scalar(pow2[:, :].bitcast(I32), amax[:, :].bitcast(I32), 0x7F800000, None,
                                 ALU.bitwise_and))
            link(v.reciprocal(w_scale[:, :], pow2[:, :]))
            link(v.tensor_scalar(u_back[:, :], w_scale[:, 0:1], 2.0 ** -20, None, ALU.mult))
            link(v.tensor_scalar(w_scale[:, :], w_scale[:, :], 2.0 ** 14, None, ALU.mult))
            link(v.tensor_scalar(g_back[:, :], pow2[:, 0:1], 2.0 ** -24, None, ALU.mult))
            link(v.scalar_tensor_tensor(out=y_back[:, :], in0=pow2[:, 0:1], scalar=2.0 ** -7,
                                        in1=pow2[:, 1:2], op0=ALU.mult, op1=ALU.mult))
            link(v.tensor_tensor(y_back[:, :], y_back[:, :], pow2[:, 2:3], ALU.mult))
            for step in range(4):
                unpack(0, -6, step)

            dve.wait_ge(consts, 13)
            half_lb = LB // 2
            for f in range(2):
                rows = slice(half_lb * B * f, half_lb * B * (f + 1))
                dve.wait_ge(gram_done, f + 1)
                v.tensor_tensor(masked[:, rows, :], gram[:, half_lb * f:half_lb * (f + 1), :, :]
                                .rearrange("p b m l -> p (b m) l"),
                                mask32[:, None, :].broadcast_to([P, half_lb * B, 32]),
                                ALU.mult).then_inc(gram_read, 1)
                dve.wait_ge(gram_read, f + 1)
                link(v.tensor_reduce(scores[:, half_lb * f:half_lb * (f + 1), :]
                                     .rearrange("p b m -> p (b m)"), masked[:, rows, :], AX, ALU.add))
            link(v.tensor_reduce(row_stat[:, :], scores[:, :, :], AX, ALU.max))
            v.tensor_tensor(scores[:, :, :], scores[:, :, :],
                            row_stat[:, :, None].broadcast_to([P, LB, B]), ALU.subtract).then_inc(diff_ready, 1)
            dve.wait_ge(exp_ready, 1)
            link(v.tensor_reduce(row_stat[:, :], prob[:, :, :], AX, ALU.add))
            link(v.reciprocal(row_stat[:, :], row_stat[:, :]))
            v.tensor_tensor(prob[:, :, :], prob[:, :, :],
                            row_stat[:, :, None].broadcast_to([P, LB, B]), ALU.mult).then_inc(prob_ready, 1)
            dve.wait_ge(rep_done, 1)
            for m in range(B):
                rows = slice(32 * m, 32 * m + 32)
                v.tensor_tensor(prob_m[rows, :, :],
                                ps[rows, 4, :].rearrange("p (n b m) -> p b n m", n=B, m=B)[:, :, :, m],
                                same_n[rows, None, :].broadcast_to([32, LB, B]), ALU.add).then_inc(v_chain, 1)
                chained[0] += 1
            dve.wait_ge(v_chain, chained[0])
            for f in range(2):
                rows = slice(half_lb * f, half_lb * (f + 1))
                v.tensor_tensor(d_mat[:, rows, :, :].rearrange("p b n l -> p (b n) l"),
                                prob_m[:, rows, :].rearrange("p b n -> p (b n)")[:, :, None]
                                .broadcast_to([P, half_lb * B, 32]),
                                mask32[:, None, :].broadcast_to([P, half_lb * B, 32]),
                                ALU.mult).then_inc(d_ready, 1)

            def add_message(ct, g):
                k = LG * ct + g
                dve.wait_ge(m_done, k + 1)
                dst = acc[:, B * ct:B * ct + B, P * g:P * g + P]
                v.tensor_tensor(dst, ps[:, 2 + k % 2, :].rearrange("p (n l) -> p n l", n=B), dst,
                                ALU.add).then_inc(x1_ready, 1)

            def x_low(k):
                j, f = k // 2, k % 2
                dst = xn_t[j // B][:, :, 4 * f:4 * f + 4, (j % B) * P:(j % B) * P + P]
                dve.wait_ge(xhi_done, k + 1)
                v.tensor_tensor(dst[:, 1], ps[:, 4 + k % 4, :].rearrange("p (k c) -> p k c", c=P),
                                dst[:, 0], ALU.subtract).then_inc(xlo_done, 1)

            ahead = [(j, step) for j in (-6, -5, -4, -3) for step in range(9)][4:]
            for g in range(LG):
                add_message(0, g)
                unpack(0, *ahead[g])
            for ct in (1, 2):
                dve.wait_ge(x1_ready, LG * ct)
                for g in range(LG):
                    add_message(ct, g)
                    row_stats(CT + ct - 1, g)
                row_sums(CT + ct - 1)
            for half in range(2 * B):
                x_low(half)
                if half % 2:
                    unpack(0, *ahead[LG + half // 2])
            dve.wait_ge(x1_ready, 3 * LG)
            for g in range(LG):
                add_message(3, g)
                row_stats(CT + 2, g)
            row_sums(CT + 2)
            for half in range(2 * B):
                x_low(2 * B + half)
                if half % 2:
                    unpack(0, *ahead[LG + 4 + half // 2])
            for half in range(2 * B):
                x_low(4 * B + half)
                unpack(0, *ahead[LG + 8 + half])
            for j, step in ahead[2 * LG + 8:]:
                unpack(0, j, step)
            low_part(0, -3)
            dve.wait_ge(x1_ready, CT * LG)
            for half in range(2 * B):
                row_stats(CT + 3, half)
            row_sums(CT + 3)
            for step in range(9):
                if step != 6:
                    unpack(0, -2, step)
            for half in range(2 * B):
                x_low(6 * B + half)
            unpack_half(0, -1)

            def chunk(i, with_pair=WITH_PAIR, until=NBODY):
                for j in range(with_pair[0][0]):
                    unpack_half(i, j)
                for p in range(PAIRS):
                    h_product(i, p)
                    for at, j in enumerate(with_pair[p]):
                        for step in range(9):
                            if j < until:
                                unpack(i, j, step)
                            elif j == until and step == 0:
                                low_part(i, j - 1)
                            if at == 0 and step == 2:
                                h_low(i, p)
                    if not with_pair[p]:
                        h_low(i, p)
                left = 9 * max(0, until - 1 - with_pair[-2][-1])
                done = 0
                for a in range(ADDS):
                    add(i, a)
                    while done < (a + 1) * left // ADDS:
                        unpack(i, with_pair[-2][-1] + 1 + done // 9, done % 9)
                        done += 1

            chunk(0, WITH_PAIR_FIRST)
            with dve.Fori(1, NCHUNK - 1) as i:
                chunk(i)
            chunk(NCHUNK - 1, until=NLAST)

        @block.tensor
        def _(pe):
            mm = nc.tensor.matmul
            for ct in range(CT):
                pe.wait_ge(y_act, 2 * (ct + 1))
                pe.wait_ge(y_pool, ct + 1)
                pe.wait_ge(y_dve, ct + 1)
                for lb in range(LB):
                    cols = y_nat[ct][:, lb, :, :].rearrange("p n l -> p (n l)")
                    last = mm(gram[:, lb, :, :], cols, cols, start=(ct == 0 and lb % 4 == 0),
                              stop=(ct == CT - 1), skip_group_check=True)
                    if ct == CT - 1 and lb in (LB // 2 - 1, LB - 1):
                        last.then_inc(gram_done, 1)

            def transpose_y(ct, g):
                k = LG * ct + g
                if k == 0:
                    pe.wait_ge(consts, 13)
                    pe.wait_ge(gram_read, 1)
                elif k >= 2:
                    pe.wait_ge(t_read, k - 1)
                for b in range(4):
                    lb = 4 * g + b
                    last = nc.tensor.transpose(ps[:, k % 2, P * b:P * b + P],
                                               y_nat[ct][:, lb, :, :].rearrange("p n l -> p (n l)"), ident[:, :])
                last.then_inc(t_done, 1)

            def messages(ct, g):
                k = LG * ct + g
                pe.wait_ge(t_read, k + 1)
                if ct == 0:
                    pe.wait_ge(d_ready, 1 + g // (LG // 2))
                if k >= 2:
                    pe.wait_ge(x1_ready, k - 1)
                bank = ps[:, 2 + k % 2, :].rearrange("p (n b l) -> p n b l", n=B, l=32)
                for b in range(4):
                    lb = 4 * g + b
                    last = mm(bank[:, :, b, :], y_t[:, lb, :], d_mat[:, lb, :, :], start=True, stop=True)
                last.then_inc(m_done, 1)

            def transpose_xn(ct):
                for k in range(2 * B * ct, 2 * B * (ct + 1)):
                    pe.wait_ge(xn_ready, k + 1)
                    if k >= 4:
                        pe.wait_ge(xlo_done, k - 3)
                    for b in range(4):
                        last = nc.tensor.transpose(ps[:, 4 + k % 4, P * b:P * b + P],
                                                   xn_buf[:, k % 2, P * b:P * b + P], ident[:, :])
                    last.then_inc(t2_done, 1)

            def gate_up(i, p):
                n = PAIRS * i + p
                mt, ct = p // CT, p % CT
                for g, bank, ready, read in ((0, p % 2, gate_ready, gate_read), (1, 2 + p % 2, up_ready, up_read)):
                    if ct == 0:
                        pe.wait_ge(los_done, NBODY * i + 4 * mt + 2 * g + 2)
                    if not (isinstance(n, int) and n < 2):
                        pe.wait_ge(read, n - 1)
                    w = gu_w[mt][:, g]
                    for kt in range(KT):
                        hi, lo = w[:, 0, P * kt:P * kt + P], w[:, 1, P * kt:P * kt + P]
                        mm(ps[:, bank, :], hi, xn_t[ct][:, 0, kt, :], start=(kt == 0), stop=False)
                        mm(ps[:, bank, :], hi, xn_t[ct][:, 1, kt, :], start=False, stop=False)
                        last = mm(ps[:, bank, :], lo, xn_t[ct][:, 0, kt, :], start=False, stop=(kt == KT - 1))
                    last.then_inc(ready, 1)

            def down(i, t):
                if t == 0:
                    pe.wait_ge(los_done, NBODY * i + NA + 6)
                if t % B == 0:
                    pe.wait_ge(hlo_done, PAIRS * i + PAIRS - CT + t // B + 1)
                for f in range(2):
                    a = 2 * t + f
                    n = ADDS * i + a
                    if not (isinstance(n, int) and n < 4):
                        pe.wait_ge(down_added, n - 3)
                for mt in range(CM):
                    for part, sides in ((0, (0, 1)), (1, (2,))):
                        for s in sides:
                            for f in range(2):
                                a = 2 * t + f
                                last = mm(ps[:, 4 + a % 4, :], h_hl[:, mt, part, P * t:P * t + P],
                                          down_w[:, mt, s, 512 * f:512 * f + 512],
                                          start=(mt == 0 and part == 0 and s == 0),
                                          stop=(mt == CM - 1 and part == 1))
                                if mt == CM - 1 and part == 1:
                                    last.then_inc(down_ready, 1)

            for g in range(LG):
                transpose_y(0, g)
            pe.wait_ge(prob_ready, 1)
            pe.wait_ge(gram_read, 2)
            for n in range(B):
                last = mm(ps[:, 4, P * n:P * n + P], rep[:, n, :], prob[:, :, :], start=True, stop=True)
            last.then_inc(rep_done, 1)
            for ct in range(CT):
                for g in range(LG):
                    messages(ct, g)
                    if ct + 1 < CT:
                        transpose_y(ct + 1, g)
                if ct >= 2:
                    transpose_xn(ct - 2)
            transpose_xn(2)
            pe.wait_ge(xlo_done, 2 * B)
            pe.wait_ge(x1_ready, CT * LG)
            gate_up(0, 0)
            transpose_xn(3)
            for i, p in ((0, p) for p in range(1, PAIRS)):
                if p < CT:
                    pe.wait_ge(xlo_done, 2 * B * (p + 1))
                gate_up(i, p)
            for t in range(NJ):
                down(0, t)
            with pe.Fori(1, NCHUNK - 1) as i:
                for p in range(PAIRS):
                    gate_up(i, p)
                for t in range(NJ):
                    down(i, t)
            for p in range(PAIRS):
                gate_up(NCHUNK - 1, p)
            for t in range(NJ):
                down(NCHUNK - 1, t)


def stream_order():
    for mat, mt, half, _ in AHEAD:
        yield mat, mt, half
    for i in range(NCHUNK):
        for mat, mt, half, nxt in (BODY if i < NCHUNK - 1 else BODY[:NLAST]):
            yield mat, CM * (i + nxt) + mt, half


def kernel(L0_attn_x, L0_ffn_gate_q, L0_ffn_gate_absmax, L0_ffn_up_q, L0_ffn_up_absmax,
           L0_ffn_down_q, L0_ffn_down_absmax):
    import numpy as np
    import concourse.bacc as bacc
    from concourse.bass_utils import run_bass_kernel_spmd

    x = np.ascontiguousarray(L0_attn_x)
    q = [np.asarray(L0_ffn_gate_q), np.asarray(L0_ffn_up_q), np.asarray(L0_ffn_down_q)]
    a = [np.asarray(v) for v in (L0_ffn_gate_absmax, L0_ffn_up_absmax, L0_ffn_down_absmax)]
    absmax = np.stack(a)
    q_half, a_half = [], []
    for mat in (0, 1):
        q_half.append(q[mat].reshape(M // P, P, 2, KT // 2, P).transpose(0, 2, 4, 3, 1)
                      .reshape(M // P, 2, P, HALF))
        a_half.append(a[mat].reshape(M // P, P, 2, KT // 2, 2).transpose(0, 2, 4, 3, 1)
                      .reshape(M // P, 2, 2, HALF))
    q_half.append(q[2].reshape(2, HALF, M // P, P).transpose(2, 0, 3, 1))
    a_half.append(a[2].reshape(2, HALF, M // P, 2).transpose(2, 0, 3, 1))
    order = list(stream_order())
    q_stream = np.stack([q_half[mat][mt, half] for mat, mt, half in order])
    a_stream = np.stack([a_half[mat][mt, half] for mat, mt, half in order])

    nc = bacc.Bacc("TRN2", target_bir_lowering=False, num_devices=1)
    arrays = {"x_dram": x, "q_dram": q_stream, "a_dram": a_stream, "absmax_dram": absmax}
    args = [nc.dram_tensor(n, v.shape, mybir.dt.from_np(v.dtype), kind="ExternalInput").ap()
            for n, v in arrays.items()]
    args.append(nc.dram_tensor("out_dram", x.shape, mybir.dt.from_np(x.dtype), kind="ExternalOutput").ap())
    block_kernel(nc, *args)
    return run_bass_kernel_spmd(nc, [arrays], core_ids=[0]).results[0]["out_dram"]
```
